# Optimizing a Trainium2 kernel written in Bass

```python
import numpy as np
import jax
import jax.numpy as jnp

def _softmax(x, axis=-1):
    return jax.nn.softmax(x, axis=axis)

def _gelu(x):
    return jax.nn.gelu(x, approximate=True)

def _silu(x):
    return jax.nn.silu(x)

def _sigmoid(x):
    return jax.nn.sigmoid(x)

def _layernorm(x, axis=-1, eps=1e-05):
    m = jnp.mean(x, axis=axis, keepdims=True)
    v = jnp.var(x, axis=axis, keepdims=True)
    return (x - m) / jnp.sqrt(v + eps)

def _scatter_add(tgt, idx, src, axis=0):
    return tgt.at[idx].add(src)

def _segment_sum(src, seg, n):
    return jax.ops.segment_sum(src, seg, n)
kernel_name = 'mk_dlrm_tower_d1_rec_r8_3bb28a'

def setup_inputs(seed: int=0):
    np.random.seed(seed)
    _w = jnp.asarray

    def _rec_inputs():
        import jax
        import jax.numpy as jnp
        _tk = jax.random.key(seed)
        dense_ctx = jax.random.normal(jax.random.fold_in(_tk, 190), (512, 16), jnp.float32)
        ids = jnp.stack([jax.random.randint(jax.random.fold_in(_tk, 200 + f), (512,), 0, v, jnp.int32) for f, v in enumerate([12500, 1000, 1250, 12500, 1250, 1000, 1250, 1000, 1000, 1250, 1000, 1250, 12500, 1250, 1250, 1000, 1250, 1250, 1250, 12500, 12500, 1250, 1000, 1250, 12500, 1250, 1000, 1000, 1000, 12500, 12500, 1250])], axis=1)
        tbl_0 = 0.05 * jax.random.normal(jax.random.fold_in(_tk, 500 + 0), (12500, 256), jnp.float32)
        tbl_1 = 0.05 * jax.random.normal(jax.random.fold_in(_tk, 500 + 1), (1000, 256), jnp.float32)
        tbl_2 = 0.05 * jax.random.normal(jax.random.fold_in(_tk, 500 + 2), (1250, 256), jnp.float32)
        tbl_3 = 0.05 * jax.random.normal(jax.random.fold_in(_tk, 500 + 3), (12500, 256), jnp.float32)
        tbl_4 = 0.05 * jax.random.normal(jax.random.fold_in(_tk, 500 + 4), (1250, 256), jnp.float32)
        tbl_5 = 0.05 * jax.random.normal(jax.random.fold_in(_tk, 500 + 5), (1000, 256), jnp.float32)
        tbl_6 = 0.05 * jax.random.normal(jax.random.fold_in(_tk, 500 + 6), (1250, 256), jnp.float32)
        tbl_7 = 0.05 * jax.random.normal(jax.random.fold_in(_tk, 500 + 7), (1000, 256), jnp.float32)
        tbl_8 = 0.05 * jax.random.normal(jax.random.fold_in(_tk, 500 + 8), (1000, 256), jnp.float32)
        tbl_9 = 0.05 * jax.random.normal(jax.random.fold_in(_tk, 500 + 9), (1250, 256), jnp.float32)
        tbl_10 = 0.05 * jax.random.normal(jax.random.fold_in(_tk, 500 + 10), (1000, 256), jnp.float32)
        tbl_11 = 0.05 * jax.random.normal(jax.random.fold_in(_tk, 500 + 11), (1250, 256), jnp.float32)
        tbl_12 = 0.05 * jax.random.normal(jax.random.fold_in(_tk, 500 + 12), (12500, 256), jnp.float32)
        tbl_13 = 0.05 * jax.random.normal(jax.random.fold_in(_tk, 500 + 13), (1250, 256), jnp.float32)
        tbl_14 = 0.05 * jax.random.normal(jax.random.fold_in(_tk, 500 + 14), (1250, 256), jnp.float32)
        tbl_15 = 0.05 * jax.random.normal(jax.random.fold_in(_tk, 500 + 15), (1000, 256), jnp.float32)
        tbl_16 = 0.05 * jax.random.normal(jax.random.fold_in(_tk, 500 + 16), (1250, 256), jnp.float32)
        tbl_17 = 0.05 * jax.random.normal(jax.random.fold_in(_tk, 500 + 17), (1250, 256), jnp.float32)
        tbl_18 = 0.05 * jax.random.normal(jax.random.fold_in(_tk, 500 + 18), (1250, 256), jnp.float32)
        tbl_19 = 0.05 * jax.random.normal(jax.random.fold_in(_tk, 500 + 19), (12500, 256), jnp.float32)
        tbl_20 = 0.05 * jax.random.normal(jax.random.fold_in(_tk, 500 + 20), (12500, 256), jnp.float32)
        tbl_21 = 0.05 * jax.random.normal(jax.random.fold_in(_tk, 500 + 21), (1250, 256), jnp.float32)
        tbl_22 = 0.05 * jax.random.normal(jax.random.fold_in(_tk, 500 + 22), (1000, 256), jnp.float32)
        tbl_23 = 0.05 * jax.random.normal(jax.random.fold_in(_tk, 500 + 23), (1250, 256), jnp.float32)
        tbl_24 = 0.05 * jax.random.normal(jax.random.fold_in(_tk, 500 + 24), (12500, 256), jnp.float32)
        tbl_25 = 0.05 * jax.random.normal(jax.random.fold_in(_tk, 500 + 25), (1250, 256), jnp.float32)
        tbl_26 = 0.05 * jax.random.normal(jax.random.fold_in(_tk, 500 + 26), (1000, 256), jnp.float32)
        tbl_27 = 0.05 * jax.random.normal(jax.random.fold_in(_tk, 500 + 27), (1000, 256), jnp.float32)
        tbl_28 = 0.05 * jax.random.normal(jax.random.fold_in(_tk, 500 + 28), (1000, 256), jnp.float32)
        tbl_29 = 0.05 * jax.random.normal(jax.random.fold_in(_tk, 500 + 29), (12500, 256), jnp.float32)
        tbl_30 = 0.05 * jax.random.normal(jax.random.fold_in(_tk, 500 + 30), (12500, 256), jnp.float32)
        tbl_31 = 0.05 * jax.random.normal(jax.random.fold_in(_tk, 500 + 31), (1250, 256), jnp.float32)
        _rk = jax.random.fold_in(_tk, 7)
        W_top1 = 0.0441942 * jax.random.normal(jax.random.fold_in(_tk, 801), (512, 512), jnp.float32)
        W_top2 = 0.0441942 * jax.random.normal(jax.random.fold_in(_tk, 802), (512, 256), jnp.float32)
        W_top3 = 0.0625 * jax.random.normal(jax.random.fold_in(_tk, 803), (256, 1), jnp.float32)
        b_top1 = jnp.zeros((512,), jnp.float32)
        b_top2 = jnp.zeros((256,), jnp.float32)
        return (dense_ctx, ids, tbl_0, tbl_1, tbl_2, tbl_3, tbl_4, tbl_5, tbl_6, tbl_7, tbl_8, tbl_9, tbl_10, tbl_11, tbl_12, tbl_13, tbl_14, tbl_15, tbl_16, tbl_17, tbl_18, tbl_19, tbl_20, tbl_21, tbl_22, tbl_23, tbl_24, tbl_25, tbl_26, tbl_27, tbl_28, tbl_29, tbl_30, tbl_31, W_top1, b_top1, W_top2, b_top2, W_top3)
    dense_ctx, ids, tbl_0, tbl_1, tbl_2, tbl_3, tbl_4, tbl_5, tbl_6, tbl_7, tbl_8, tbl_9, tbl_10, tbl_11, tbl_12, tbl_13, tbl_14, tbl_15, tbl_16, tbl_17, tbl_18, tbl_19, tbl_20, tbl_21, tbl_22, tbl_23, tbl_24, tbl_25, tbl_26, tbl_27, tbl_28, tbl_29, tbl_30, tbl_31, W_top1, b_top1, W_top2, b_top2, W_top3 = _rec_inputs()

    def _L0_rec_setup():
        import jax, jax.numpy as jnp
        import numpy as np
        B, N, D = (1024, 32, 256)
        key = jax.random.key(seed)
        x = jax.random.normal(key, (B, N, D), dtype=jnp.float32)
        return {'x': x}
    _L0_rec_all = _L0_rec_setup()
    _L0_rec_in = {k: v for k, v in _L0_rec_all.items() if k in ()}
    del _L0_rec_all
    return {'dense_ctx': dense_ctx, 'ids': ids, 'tbl_0': tbl_0, 'tbl_1': tbl_1, 'tbl_2': tbl_2, 'tbl_3': tbl_3, 'tbl_4': tbl_4, 'tbl_5': tbl_5, 'tbl_6': tbl_6, 'tbl_7': tbl_7, 'tbl_8': tbl_8, 'tbl_9': tbl_9, 'tbl_10': tbl_10, 'tbl_11': tbl_11, 'tbl_12': tbl_12, 'tbl_13': tbl_13, 'tbl_14': tbl_14, 'tbl_15': tbl_15, 'tbl_16': tbl_16, 'tbl_17': tbl_17, 'tbl_18': tbl_18, 'tbl_19': tbl_19, 'tbl_20': tbl_20, 'tbl_21': tbl_21, 'tbl_22': tbl_22, 'tbl_23': tbl_23, 'tbl_24': tbl_24, 'tbl_25': tbl_25, 'tbl_26': tbl_26, 'tbl_27': tbl_27, 'tbl_28': tbl_28, 'tbl_29': tbl_29, 'tbl_30': tbl_30, 'tbl_31': tbl_31, 'W_top1': W_top1, 'b_top1': b_top1, 'W_top2': W_top2, 'b_top2': b_top2, 'W_top3': W_top3}

def reference(dense_ctx, ids, tbl_0, tbl_1, tbl_2, tbl_3, tbl_4, tbl_5, tbl_6, tbl_7, tbl_8, tbl_9, tbl_10, tbl_11, tbl_12, tbl_13, tbl_14, tbl_15, tbl_16, tbl_17, tbl_18, tbl_19, tbl_20, tbl_21, tbl_22, tbl_23, tbl_24, tbl_25, tbl_26, tbl_27, tbl_28, tbl_29, tbl_30, tbl_31, W_top1, b_top1, W_top2, b_top2, W_top3):
    import jax
    import jax.numpy as jnp

    def _L0_rec_ref(x):
        import jax, jax.numpy as jnp
        import numpy as np
        B, N, D = (1024, 32, 256)
        'Second-order feature interaction (DLRM dot interaction).\n\n            Computes dot(x_i, x_j) for all field pairs i < j (self_interaction=False),\n            flattened in row-major upper-triangular order -> [B, N*(N-1)/2].\n            Matches tf.boolean_mask(dot_products, strictly_upper_mask) ordering.\n            '
        b, n, d = x.shape
        iu, ju = jnp.triu_indices(n, k=1)
        dots = jnp.einsum('bnd,bmd->bnm', x, x)
        return dots[:, iu, ju]
    e = jnp.stack([tbl_0[ids[:, 0]], tbl_1[ids[:, 1]], tbl_2[ids[:, 2]], tbl_3[ids[:, 3]], tbl_4[ids[:, 4]], tbl_5[ids[:, 5]], tbl_6[ids[:, 6]], tbl_7[ids[:, 7]], tbl_8[ids[:, 8]], tbl_9[ids[:, 9]], tbl_10[ids[:, 10]], tbl_11[ids[:, 11]], tbl_12[ids[:, 12]], tbl_13[ids[:, 13]], tbl_14[ids[:, 14]], tbl_15[ids[:, 15]], tbl_16[ids[:, 16]], tbl_17[ids[:, 17]], tbl_18[ids[:, 18]], tbl_19[ids[:, 19]], tbl_20[ids[:, 20]], tbl_21[ids[:, 21]], tbl_22[ids[:, 22]], tbl_23[ids[:, 23]], tbl_24[ids[:, 24]], tbl_25[ids[:, 25]], tbl_26[ids[:, 26]], tbl_27[ids[:, 27]], tbl_28[ids[:, 28]], tbl_29[ids[:, 29]], tbl_30[ids[:, 30]], tbl_31[ids[:, 31]]], axis=1)
    z = _L0_rec_ref(e)
    z = z.reshape(z.shape[0], -1)
    h = jnp.concatenate([z, dense_ctx], axis=1)
    h = jnp.maximum(h @ W_top1 + b_top1, 0.0)
    h = jnp.maximum(h @ W_top2 + b_top2, 0.0)
    y = h @ W_top3
    return y

_drawn_inputs = setup_inputs


def setup_inputs(seed=0):
    import zlib

    import numpy as np

    out = dict(_drawn_inputs(seed))
    spreads = {'b_top1': (0.0, 0.1), 'b_top2': (0.0, 0.1)}
    factors = {}
    for name, (base, spread) in spreads.items():
        noise = np.random.default_rng([zlib.crc32(name.encode()), seed]).standard_normal(out[name].shape)
        drawn = base * np.exp(spread * noise) if base else spread * noise
        out[name] = jnp.asarray(drawn.astype(out[name].dtype))
    for name, factor in factors.items():
        out[name] = (out[name] * factor).astype(out[name].dtype)
    return out
```

```python
import concourse.bass as bass
from concourse import mybir
from contextlib import ExitStack

P = 128
FIELDS = 32
QUADS = P // FIELDS
HALF = FIELDS // 2


def dlrm_tower_kernel(nc: bass.Bass, table: bass.AP, ids: bass.AP, first_row: bass.AP, dense: bass.AP,
                      w1: bass.AP, b1: bass.AP, w2: bass.AP, b2: bass.AP, w3: bass.AP, y: bass.AP):
    fp32 = mybir.dt.float32
    i32 = mybir.dt.int32
    u32 = mybir.dt.uint32
    ALU = mybir.AluOpType
    ACT = mybir.ActivationFunctionType

    D = table.shape[1]
    DC = D // P
    TILES = ids.shape[1]
    DENSE = HALF
    CHUNK_TILES = FIELDS
    CHUNKS = TILES // CHUNK_TILES
    RING = 16
    BODIES = CHUNK_TILES // RING
    PAIRS = RING // 2
    GROUPS = RING // 4
    HID1 = w1.shape[1]
    HID2 = w2.shape[1]
    KC = w1.shape[0] // P
    J1 = HID1 // P
    J2 = HID2 // P
    BATCH = y.shape[1]

    ctx = ExitStack()
    with ctx:
        def sb(name, shape, dt=fp32):
            return ctx.enter_context(nc.sbuf_tensor(name, shape, dt))

        def bank(name):
            return ctx.enter_context(nc.psum_tensor(name, [P, 512], fp32))

        def sem(name):
            return ctx.enter_context(nc.semaphore(name))

        ids_sb = sb("ids_sb", [P, TILES], i32)
        base_sb = sb("base_sb", [P, 1], i32)
        rows_sb = sb("rows_sb", [P, TILES], i32)
        stage = sb("stage", [P, RING], i32)
        ring = sb("ring", [P, RING, D])
        eT = sb("eT", [P, 2, 2, DC, P])
        dots = sb("dots", [P, CHUNK_TILES, FIELDS])
        z = sb("z", [P, FIELDS, FIELDS])
        dense_sb = sb("dense_sb", [P, CHUNKS, DENSE])
        ident = sb("ident", [P, P])
        upper = sb("upper", [P, HALF, HALF])
        hT = sb("hT", [P, KC, P])
        h1T = sb("h1T", [P, J1, P])
        h2T = sb("h2T", [P, J2, P])
        w1_sb = sb("w1_sb", [P, KC, HID1])
        w2_sb = sb("w2_sb", [P, J1, HID2])
        w3_sb = sb("w3_sb", [P, J2])
        b1_sb = sb("b1_sb", [P, J1])
        b2_sb = sb("b2_sb", [P, J2])
        y_sb = sb("y_sb", [1, BATCH])

        T_ps = [bank(f"T_ps{i}") for i in range(2)]
        G_ps = [bank(f"G_ps{i}") for i in range(2)]
        M_ps = [bank(f"M_ps{i}") for i in range(4)]

        ids_in = sem("ids_in")
        dense_in = sem("dense_in")
        w1_in = sem("w1_in")
        w23_in = sem("w23_in")
        ident_zeroed = sem("ident_zeroed")
        consts_made = sem("consts_made")
        rows_made = sem("rows_made")
        staged = [sem(f"staged{i}") for i in range(2)]
        gathered = [sem(f"gathered{k}") for k in range(RING)]
        slots_taken = sem("slots_taken")
        pair_transposed = [sem(f"pair_transposed{i}") for i in range(2)]
        pair_copied = [sem(f"pair_copied{i}") for i in range(2)]
        pair_multiplied = [sem(f"pair_multiplied{i}") for i in range(2)]
        dots_copied = [sem(f"dots_copied{i}") for i in range(2)]
        z_made = sem("z_made")
        z_dense = sem("z_dense")
        z_folded = sem("z_folded")
        features_transposed = sem("features_transposed")
        features_copied = sem("features_copied")
        layer1_summed = sem("layer1_summed")
        h1_by_act = sem("h1_by_act")
        h1_by_dve = sem("h1_by_dve")
        layer2_summed = sem("layer2_summed")
        h2_by_act = sem("h2_by_act")
        h2_by_dve = sem("h2_by_dve")
        layer3_summed = sem("layer3_summed")
        y_copied = sem("y_copied")
        y_stored = sem("y_stored")

        HR = RING // 2
        FREE = 1
        block = ctx.enter_context(nc.Block())

        @block.sync
        def _(sp):
            sp.dma_start(ids_sb[:], ids).then_inc(ids_in, 16)
            sp.dma_start(base_sb[:], first_row).then_inc(ids_in, 16)
            sp.dma_start(dense_sb[:], dense.rearrange("(c p) f -> p c f", p=P)).then_inc(dense_in, 16)
            sp.wait_ge(rows_made, 2)
            with sp.Fori(1, CHUNKS * BODIES) as turn:
                for half in range(2):
                    for k in range(half * HR, (half + 1) * HR):
                        sp.wait_ge(gathered[k], turn * 16)
                    sp.dma_start(stage[:, half * HR:(half + 1) * HR],
                                 rows_sb[:, bass.ds(turn * RING + half * HR, HR)]).then_inc(staged[half], 16)
            sp.wait_ge(y_copied, FREE + CHUNKS)
            sp.dma_start(y, y_sb[:]).then_inc(y_stored, 16)
            sp.wait_ge(y_stored, 16)

        @block.gpsimd
        def _(pool):
            nc.gpsimd.memset(ident[:], 0.0).then_inc(ident_zeroed, 1)
            nc.gpsimd.memset(upper[:], 1.0).then_inc(ident_zeroed, 1)
            pool.wait_ge(ident_zeroed, 2)
            nc.gpsimd.affine_select(out=ident[:], in_=ident[:], compare_op=ALU.not_equal, fill=1.0, base=0,
                                    pattern=[[-1, P]], channel_multiplier=1).then_inc(consts_made, 1)
            nc.gpsimd.affine_select(out=upper[:], in_=upper[:], compare_op=ALU.is_ge, fill=0.0, base=0,
                                    pattern=[[-1, HALF], [1, HALF]], channel_multiplier=0).then_inc(consts_made, 1)

            def gather(k):
                nc.gpsimd.indirect_dma_start(
                    ring[:, k, :], None, table, bass.IndirectOffsetOnAxis(ap=stage[:, k:k + 1], axis=0)).then_inc(gathered[k], 16)

            pool.wait_ge(rows_made, 1)
            for k in range(RING):
                gather(k)
            with pool.Fori(1, CHUNKS * BODIES) as turn:
                for k in range(RING):
                    if k % HR == 0:
                        pool.wait_ge(staged[k // HR], turn * 16)
                    if k % 2 == 0:
                        pool.wait_ge(pair_transposed[k // 2 % 2], turn * (PAIRS // 2) - PAIRS // 2 + k // 4 + 1)
                        pool.sem_inc(slots_taken, 1)
                    gather(k)

        @block.tensor
        def _(pe):
            for done in (*pair_multiplied, features_transposed):
                pe.sem_inc(done, FREE)
            pe.wait_ge(consts_made, 2)

            def transpose_pair(turn, j):
                pe.wait_ge(pair_copied[j % 2], FREE + turn * (PAIRS // 2) + j // 2)
                for tile in range(2):
                    k = 2 * j + tile
                    pe.wait_ge(gathered[k], turn * 16 + 16)
                    for dc in range(DC):
                        at = (tile * DC + dc) * P
                        last = nc.tensor.transpose(T_ps[j % 2][:, at:at + P], ring[:, k, dc * P:(dc + 1) * P],
                                                   ident[:])
                last.then_inc(pair_transposed[j % 2], 1)

            def multiply_pair(turn, j):
                g = j // 2
                if j % 2 == 0:
                    pe.wait_ge(dots_copied[g % 2], 2 * FREE + turn * GROUPS + 2 * (g // 2))
                pe.wait_ge(pair_copied[j % 2], FREE + turn * (PAIRS // 2) + j // 2 + 1)
                for tile in range(2):
                    at = (2 * (j % 2) + tile) * P
                    for dc in range(DC):
                        e = eT[:, j % 2, tile, dc, :]
                        last = nc.tensor.matmul(G_ps[g % 2][:, at:at + P], e, e, start=(dc == 0), stop=(dc == DC - 1))
                last.then_inc(pair_multiplied[j % 2], 1)

            with pe.Fori(0, CHUNKS) as c:
                with pe.Fori(0, BODIES) as body:
                    turn = c * BODIES + body
                    transpose_pair(turn, 0)
                    for j in range(1, PAIRS):
                        transpose_pair(turn, j)
                        multiply_pair(turn, j - 1)
                    multiply_pair(turn, PAIRS - 1)

                pe.wait_ge(z_folded, c + 1)
                pe.wait_ge(y_copied, FREE + c)
                for kc in range(KC):
                    rows = HALF + kc * (P // FIELDS)
                    last = nc.tensor.transpose(M_ps[kc // 2][:, (kc % 2) * P:(kc % 2 + 1) * P],
                                               z[:, rows:rows + P // FIELDS, :], ident[:])
                    if kc % 2 == 1:
                        last.then_inc(features_transposed, 1)

                pe.wait_ge(w1_in, 32)
                pe.wait_ge(features_copied, 2 * c + 2)
                for jc in range(J1):
                    for kc in range(KC):
                        last = nc.tensor.matmul(M_ps[(jc + 2) % 4][:, 0:P], w1_sb[:, kc, jc * P:(jc + 1) * P],
                                                hT[:, kc, :], start=(kc == 0), stop=(kc == KC - 1))
                    last.then_inc(layer1_summed, 1)

                pe.wait_ge(w23_in, 64)
                for j2 in range(J2):
                    for kc in range(J1):
                        if j2 == 0:
                            pe.wait_ge(h1_by_dve if kc % 2 else h1_by_act, 2 * c + kc // 2 + 1)
                        last = nc.tensor.matmul(M_ps[2 + j2][:, 0:P], w2_sb[:, kc, j2 * P:(j2 + 1) * P],
                                                h1T[:, kc, :], start=(kc == 0), stop=(kc == J1 - 1))
                    last.then_inc(layer2_summed, 1)

                for kc in range(J2):
                    pe.wait_ge(h2_by_dve if kc % 2 else h2_by_act, c + 1)
                    last = nc.tensor.matmul(M_ps[0][0:1, 0:P], w3_sb[:, kc:kc + 1], h2T[:, kc, :],
                                            start=(kc == 0), stop=(kc == J2 - 1))
                last.then_inc(layer3_summed, 1)

        def copy_dots(eng, copy, c, body, g, quads):
            turn = c * BODIES + body
            eng.wait_ge(pair_multiplied[1], FREE + turn * (PAIRS // 2) + g + 1)
            if g == 0:
                eng.wait_ge(z_made, FREE + c)
            for q in quads:
                rows = slice(q * FIELDS, (q + 1) * FIELDS)
                src = G_ps[g % 2][rows, :].rearrange("p (t x) -> p t x", t=4)[:, :, rows]
                last = copy(dots[rows, bass.ds(body * RING + 4 * g, 4), :], src)
            last.then_inc(dots_copied[g % 2], 1)

        def copy_pair(eng, copy, turn, j):
            eng.wait_ge(pair_transposed[j % 2], turn * (PAIRS // 2) + j // 2 + 1)
            eng.wait_ge(pair_multiplied[j % 2], FREE + turn * (PAIRS // 2) + j // 2)
            copy(eT[:, j % 2].rearrange("p a b c -> p (a b c)"), T_ps[j % 2][:]).then_inc(pair_copied[j % 2], 1)

        @block.scalar
        def _(act):
            act.dma_start(w1_sb[:, 0:KC // 2], w1[0:KC // 2 * P].rearrange("(c p) j -> p c j", p=P)).then_inc(w1_in, 16)
            act.dma_start(w1_sb[:, KC // 2:KC], w1[KC // 2 * P:].rearrange("(c p) j -> p c j", p=P)).then_inc(w1_in, 16)
            act.dma_start(w2_sb[:], w2.rearrange("(c p) j -> p c j", p=P)).then_inc(w23_in, 16)
            act.dma_start(w3_sb[:], w3).then_inc(w23_in, 16)
            act.dma_start(b1_sb[:], b1).then_inc(w23_in, 16)
            act.dma_start(b2_sb[:], b2).then_inc(w23_in, 16)

            for done in (pair_copied[1], *dots_copied):
                act.sem_inc(done, FREE)
            with act.Fori(0, CHUNKS) as c:
                with act.Fori(0, BODIES) as body:
                    turn = c * BODIES + body
                    for j in range(1, PAIRS, 2):
                        copy_pair(act, nc.scalar.copy, turn, j)
                        if j >= 3:
                            copy_dots(act, nc.scalar.copy, c, body, j // 2 - 1, (2, 3))
                    copy_dots(act, nc.scalar.copy, c, body, GROUPS - 1, (2, 3))

                act.wait_ge(features_transposed, FREE + 2 * c + 2)
                nc.scalar.copy(hT[:, KC // 2:KC, :], M_ps[1][:, 0:KC // 2 * P]).then_inc(features_copied, 1)
                act.wait_ge(w23_in, 64)
                for jc in range(0, J1, 2):
                    act.wait_ge(layer1_summed, J1 * c + jc + 1)
                    nc.scalar.activation(h1T[:, jc, :], M_ps[(jc + 2) % 4][:, 0:P], ACT.Relu,
                                         bias=b1_sb[:, jc:jc + 1]).then_inc(h1_by_act, 1)
                act.wait_ge(layer2_summed, J2 * c + 1)
                nc.scalar.activation(h2T[:, 0, :], M_ps[2][:, 0:P], ACT.Relu, bias=b2_sb[:, 0:1]).then_inc(h2_by_act, 1)

        @block.vector
        def _(dve):
            for done in (pair_copied[0], *dots_copied, z_made, y_copied):
                dve.sem_inc(done, FREE)
            dve.wait_ge(ids_in, 32)
            nc.vector.tensor_scalar(stage[:], ids_sb[:, 0:RING], base_sb[:, 0:1], None, ALU.add).then_inc(rows_made, 1)
            nc.vector.tensor_scalar(rows_sb[:], ids_sb[:], base_sb[:, 0:1], None, ALU.add).then_inc(rows_made, 1)

            with dve.Fori(0, CHUNKS) as c:
                with dve.Fori(0, BODIES) as body:
                    turn = c * BODIES + body
                    for j in range(0, PAIRS, 2):
                        copy_pair(dve, nc.vector.tensor_copy, turn, j)
                        if j >= 2:
                            copy_dots(dve, nc.vector.tensor_copy, c, body, j // 2 - 1, (0, 1))
                    copy_dots(dve, nc.vector.tensor_copy, c, body, GROUPS - 1, (0, 1))

                for b in range(2):
                    dve.wait_ge(dots_copied[b], 2 * FREE + (c + 1) * (BODIES * GROUPS))
                dve.wait_ge(features_transposed, FREE + 2 * c)
                nc.vector.transpose(z[:], dots[:].rearrange("p t m -> p m t")).then_inc(z_made, 1)
                dve.wait_ge(z_made, FREE + c + 1)
                dve.wait_ge(dense_in, 16)
                diag = z[:].rearrange("p m n -> p (m n)")[:, 0:(HALF - 1) * (FIELDS + 1) + 1:FIELDS + 1]
                nc.vector.tensor_copy(diag, dense_sb[:, bass.ds(c, 1), :]).then_inc(z_dense, 1)
                dve.wait_ge(consts_made, 2)
                dve.wait_ge(z_dense, c + 1)
                nc.vector.copy_predicated(z[:, HALF:, HALF:], upper[:].bitcast(u32),
                                          z[:, 0:HALF, 0:HALF]).then_inc(z_folded, 1)

                dve.wait_ge(features_transposed, FREE + 2 * c + 1)
                nc.vector.tensor_copy(hT[:, 0:KC // 2, :], M_ps[0][:, 0:KC // 2 * P]).then_inc(features_copied, 1)
                dve.wait_ge(w23_in, 64)
                for jc in range(1, J1, 2):
                    dve.wait_ge(layer1_summed, J1 * c + jc + 1)
                    nc.vector.tensor_scalar(h1T[:, jc, :], M_ps[(jc + 2) % 4][:, 0:P], b1_sb[:, jc:jc + 1], 0.0,
                                            ALU.add, ALU.max).then_inc(h1_by_dve, 1)
                dve.wait_ge(layer2_summed, J2 * c + 2)
                nc.vector.tensor_scalar(h2T[:, 1, :], M_ps[3][:, 0:P], b2_sb[:, 1:2], 0.0,
                                        ALU.add, ALU.max).then_inc(h2_by_dve, 1)
                dve.wait_ge(layer3_summed, c + 1)
                nc.vector.tensor_copy(y_sb[:, bass.ts(c, P)], M_ps[0][0:1, 0:P]).then_inc(y_copied, 1)


def feature_rows(fields, half, dense):
    import numpy as np

    pair = np.zeros((fields, fields), np.int64)
    iu, ju = np.triu_indices(fields, k=1)
    pair[iu, ju] = np.arange(len(iu))
    pair[ju, iu] = np.arange(len(iu))
    rows = pair[half:, :].copy()
    for m in range(half):
        rows[m, half + m] = len(iu) + m
        rows[m, half + m + 1:] = pair[m, m + 1:half]
    return rows.reshape(-1)


def kernel(**inputs):
    import numpy as _np
    import concourse.bacc as _bacc
    from concourse import mybir as _mybir
    from concourse.bass_utils import run_bass_kernel_spmd as _run

    tables = [_np.asarray(inputs[f"tbl_{f}"]) for f in range(FIELDS)]
    starts = _np.cumsum([0] + [t.shape[0] for t in tables[:-1]]).astype(_np.int32)
    ids = _np.asarray(inputs["ids"])
    chunks = ids.shape[0] // P
    arrays = {
        "table": _np.concatenate(tables, axis=0),
        "ids": _np.ascontiguousarray(ids.reshape(chunks, QUADS, P // QUADS, FIELDS).transpose(1, 3, 0, 2).reshape(P, -1)),
        "first_row": _np.tile(starts, QUADS).reshape(P, 1),
        "dense": _np.asarray(inputs["dense_ctx"]),
        "w1": _np.asarray(inputs["W_top1"])[feature_rows(FIELDS, HALF, HALF)],
        "b1": _np.ascontiguousarray(_np.asarray(inputs["b_top1"]).reshape(-1, P).T),
        "w2": _np.asarray(inputs["W_top2"]),
        "b2": _np.ascontiguousarray(_np.asarray(inputs["b_top2"]).reshape(-1, P).T),
        "w3": _np.ascontiguousarray(_np.asarray(inputs["W_top3"]).reshape(-1, P).T),
    }
    nc = _bacc.Bacc("TRN2", target_bir_lowering=False, num_devices=1)
    args = [nc.dram_tensor(n, a.shape, _mybir.dt.from_np(a.dtype), kind="ExternalInput").ap() for n, a in arrays.items()]
    out = nc.dram_tensor("y", (1, ids.shape[0]), _mybir.dt.float32, kind="ExternalOutput").ap()
    dlrm_tower_kernel(nc, *args, out)
    r = _run(nc, [arrays], core_ids=[0])
    return _np.asarray(r.results[0]["y"]).reshape(-1, 1)
```

```python
import concourse.bass as bass
from concourse import mybir
from contextlib import ExitStack

P = 128
FIELDS = 32
HALF = FIELDS // 2
QUADS = P // FIELDS
TILES_U = 16
UNIT = QUADS * TILES_U


def dlrm_tower_kernel(nc: bass.Bass, table: bass.AP, ids: bass.AP, first_row: bass.AP, dense: bass.AP,
                      masks: bass.AP, w1: bass.AP, b1: bass.AP, w2: bass.AP, b2: bass.AP, w3: bass.AP, y: bass.AP):
    fp32 = mybir.dt.float32
    i32 = mybir.dt.int32
    ALU = mybir.AluOpType
    ACT = mybir.ActivationFunctionType

    D = table.shape[1]
    DC = D // P
    TILES = ids.shape[1]
    UNITS = TILES // TILES_U
    PAIRS = TILES_U // 2
    GROUPS = TILES_U // 4
    MH = FIELDS // 2
    HID1 = w1.shape[1]
    HID2 = w2.shape[1]
    KC = w1.shape[0] // P
    FT = KC // 2
    J1 = HID1 // P
    J2 = HID2 // P
    BATCH = y.shape[1]

    ctx = ExitStack()
    with ctx:
        def sb(name, shape, dt=fp32):
            return ctx.enter_context(nc.sbuf_tensor(name, shape, dt))

        def bank(name):
            return ctx.enter_context(nc.psum_tensor(name, [P, 512], fp32))

        def sem(name):
            return ctx.enter_context(nc.semaphore(name))

        ids_sb = sb("ids_sb", [P, TILES], i32)
        base_sb = sb("base_sb", [P, 1], i32)
        rows_sb = sb("rows_sb", [P, TILES], i32)
        stage = sb("stage", [P, TILES_U], i32)
        ring = sb("ring", [P, TILES_U, D])
        eT = sb("eT", [P, 2, 2, DC, P])
        dots = sb("dots", [P, TILES_U, FIELDS])
        z = sb("z", [P, MH, FIELDS])
        dense_sb = sb("dense_sb", [P, UNITS, HALF])
        dense_now = sb("dense_now", [P, 1, HALF])
        masks_sb = sb("masks_sb", [P, 2, HALF // 2, HALF], i32)
        ident = sb("ident", [P, P])
        hT = sb("hT", [P, FT, 2, UNIT])
        h1T = sb("h1T", [P, J1, UNIT])
        h2T = sb("h2T", [P, J2, UNIT])
        w1_sb = sb("w1_sb", [P, KC, HID1])
        w2_sb = sb("w2_sb", [P, J1, HID2])
        w3_sb = sb("w3_sb", [P, J2])
        b1_sb = sb("b1_sb", [P, J1])
        b2_sb = sb("b2_sb", [P, J2])
        y_sb = sb("y_sb", [1, BATCH])

        T_ps = [bank(f"T_ps{i}") for i in range(2)]
        G_ps = [bank(f"G_ps{i}") for i in range(2)]
        M_ps = [bank(f"M_ps{i}") for i in range(4)]

        def l1_bank(jc):
            return M_ps[(jc + FT) % 4]

        def l2_bank(j2):
            return M_ps[2 + j2]

        out_bank = l2_bank(0)

        ids_first_in = sem("ids_first_in")
        ids_in = sem("ids_in")
        base_in = sem("base_in")
        dense_in = sem("dense_in")
        masks_in = sem("masks_in")
        w1_in = sem("w1_in")
        w23_in = sem("w23_in")
        ident_zeroed = sem("ident_zeroed")
        ident_made = sem("ident_made")
        rows_made = sem("rows_made")
        staged = [sem(f"staged{i}") for i in range(2)]
        gathered = [sem(f"gathered{k}") for k in range(TILES_U)]
        slots_taken = sem("slots_taken")
        pair_transposed = [sem(f"pair_transposed{i}") for i in range(2)]
        pair_copied = [sem(f"pair_copied{i}") for i in range(2)]
        pair_multiplied = [sem(f"pair_multiplied{i}") for i in range(2)]
        dots_copied = [sem(f"dots_copied{i}") for i in range(2)]
        dense_copied = sem("dense_copied")
        z_made = sem("z_made")
        z_dense = sem("z_dense")
        fold_steps = sem("fold_steps")
        z_folded = sem("z_folded")
        features_transposed = sem("features_transposed")
        features_copied = sem("features_copied")
        layer1_summed = sem("layer1_summed")
        h1_by_act = sem("h1_by_act")
        h1_by_dve = sem("h1_by_dve")
        layer2_summed = sem("layer2_summed")
        h2_by_act = sem("h2_by_act")
        h2_by_dve = sem("h2_by_dve")
        layer3_summed = sem("layer3_summed")
        y_copied = sem("y_copied")
        y_stored = sem("y_stored")

        FREE = 1
        PP = PAIRS // 2
        GP = GROUPS // 2
        SH = TILES_U // 2
        LAYER2, LAYER3, FEATURES, LAYER1_LOW, LAYER1_HIGH = range(5)

        block = ctx.enter_context(nc.Block())

        @block.sync
        def _(sp):
            sp.dma_start(ids_sb[:, 0:TILES_U], ids[:, 0:TILES_U]).then_inc(ids_first_in, 16)
            sp.dma_start(ids_sb[:, TILES_U:], ids[:, TILES_U:]).then_inc(ids_in, 16)
            sp.dma_start(dense_sb[:], dense.rearrange("p (u f) -> p u f", u=UNITS)).then_inc(dense_in, 16)
            sp.dma_start(masks_sb[:].rearrange("p a m n -> p (a m n)"), masks).then_inc(masks_in, 16)
            sp.wait_ge(rows_made, 2)
            with sp.Fori(1, UNITS) as u:
                for half in range(2):
                    for k in range(half * SH, (half + 1) * SH):
                        sp.wait_ge(gathered[k], u * 16)
                    sp.dma_start(stage[:, half * SH:(half + 1) * SH],
                                 rows_sb[:, bass.ds(u * TILES_U + half * SH, SH)]).then_inc(staged[half], 16)
            sp.wait_ge(y_copied, FREE + UNITS)
            sp.dma_start(y, y_sb[:]).then_inc(y_stored, 16)
            sp.wait_ge(y_stored, 16)

        @block.gpsimd
        def _(pool):
            nc.gpsimd.memset(ident[:], 0.0).then_inc(ident_zeroed, 1)
            pool.wait_ge(ident_zeroed, 1)
            nc.gpsimd.affine_select(out=ident[:], in_=ident[:], compare_op=ALU.not_equal, fill=1.0, base=0,
                                    pattern=[[-1, P]], channel_multiplier=1).then_inc(ident_made, 1)

            def gather(k):
                nc.gpsimd.indirect_dma_start(
                    ring[:, k, :], None, table,
                    bass.IndirectOffsetOnAxis(ap=stage[:, k:k + 1], axis=0)).then_inc(gathered[k], 16)

            pool.wait_ge(rows_made, 1)
            for k in range(TILES_U):
                gather(k)
            with pool.Fori(1, UNITS) as u:
                for k in range(TILES_U):
                    if k % SH == 0:
                        pool.wait_ge(staged[k // SH], u * 16)
                    if k % 2 == 0:
                        pool.wait_ge(pair_transposed[k // 2 % 2], u * PP - PP + k // 4 + 1)
                        pool.sem_inc(slots_taken, 1)
                    gather(k)

        @block.tensor
        def _(pe):
            for done in (*pair_multiplied, features_transposed):
                pe.sem_inc(done, FREE)
            pe.wait_ge(ident_made, 1)

            def transpose_pair(u, j):
                pe.wait_ge(pair_copied[j % 2], FREE + u * PP + j // 2)
                for tile in range(2):
                    k = 2 * j + tile
                    pe.wait_ge(gathered[k], u * 16 + 16)
                    for dc in range(DC):
                        at = (tile * DC + dc) * P
                        last = nc.tensor.transpose(T_ps[j % 2][:, at:at + P], ring[:, k, dc * P:(dc + 1) * P],
                                                   ident[:])
                last.then_inc(pair_transposed[j % 2], 1)

            def multiply_pair(u, j):
                g = j // 2
                if j % 2 == 0:
                    pe.wait_ge(dots_copied[g % 2], 2 * (FREE + u * GP + g // 2))
                pe.wait_ge(pair_copied[j % 2], FREE + u * PP + j // 2 + 1)
                for tile in range(2):
                    at = (2 * (j % 2) + tile) * P
                    for dc in range(DC):
                        e = eT[:, j % 2, tile, dc, :]
                        last = nc.tensor.matmul(G_ps[g % 2][:, at:at + P], e, e, start=(dc == 0), stop=(dc == DC - 1))
                last.then_inc(pair_multiplied[j % 2], 1)

            def mlp_step(u, step):
                if step == FEATURES:
                    pe.wait_ge(z_folded, u + 1)
                    for a in range(FT):
                        rows = MH // 2 + a * QUADS
                        nc.tensor.transpose(M_ps[a][:, 0:P], z[:, rows:rows + QUADS, :],
                                            ident[:]).then_inc(features_transposed, 1)
                if step == LAYER1_LOW:
                    pe.wait_ge(w1_in, 32)
                    pe.wait_ge(features_copied, 2 * u + 2)
                    pe.wait_ge(y_copied, FREE + u)
                if step in (LAYER1_LOW, LAYER1_HIGH):
                    for jc in range(J1 // 2) if step == LAYER1_LOW else range(J1 // 2, J1):
                        for kc in range(KC):
                            last = nc.tensor.matmul(l1_bank(jc)[:, 0:UNIT], w1_sb[:, kc, jc * P:(jc + 1) * P],
                                                    hT[:, kc // 2, kc % 2, :], start=(kc == 0), stop=(kc == KC - 1))
                        last.then_inc(layer1_summed, 1)
                if step == LAYER2:
                    pe.wait_ge(w23_in, 64)
                    for j2 in range(J2):
                        for kc in range(J1):
                            if j2 == 0:
                                pe.wait_ge(h1_by_dve if kc % 2 else h1_by_act, 2 * u + kc // 2 + 1)
                            last = nc.tensor.matmul(l2_bank(j2)[:, 0:UNIT], w2_sb[:, kc, j2 * P:(j2 + 1) * P],
                                                    h1T[:, kc, :], start=(kc == 0), stop=(kc == J1 - 1))
                        last.then_inc(layer2_summed, 1)
                if step == LAYER3:
                    for kc in range(J2):
                        pe.wait_ge(h2_by_dve if kc % 2 else h2_by_act, u + 1)
                        last = nc.tensor.matmul(out_bank[0:1, 0:UNIT], w3_sb[:, kc:kc + 1], h2T[:, kc, :],
                                                start=(kc == 0), stop=(kc == J2 - 1))
                    last.then_inc(layer3_summed, 1)

            def unit(u, one_before=True, two_before=True):
                for j in range(PAIRS):
                    transpose_pair(u, j)
                    if j >= 1:
                        multiply_pair(u, j - 1)
                    elif one_before:
                        multiply_pair(u - 1, PAIRS - 1)
                    if j in (LAYER2, LAYER3):
                        if two_before:
                            mlp_step(u - 2, j)
                    elif one_before:
                        mlp_step(u - 1, j)

            unit(0, one_before=False, two_before=False)
            unit(1, two_before=False)
            with pe.Fori(2, UNITS) as u:
                unit(u)
            multiply_pair(UNITS - 1, PAIRS - 1)
            mlp_step(UNITS - 2, LAYER2)
            mlp_step(UNITS - 1, FEATURES)
            mlp_step(UNITS - 2, LAYER3)
            for step in (LAYER1_LOW, LAYER1_HIGH, LAYER2, LAYER3):
                mlp_step(UNITS - 1, step)

        def copy_dots(eng, copy, u, g, quads):
            eng.wait_ge(pair_multiplied[1], FREE + u * PP + g + 1)
            if g == 0:
                eng.wait_ge(z_made, FREE + u)
            for q in quads:
                rows = slice(q * FIELDS, (q + 1) * FIELDS)
                src = G_ps[g % 2][rows, :].rearrange("p (t x) -> p t x", t=4)[:, :, rows]
                last = copy(dots[rows, 4 * g:4 * g + 4, :], src)
            last.then_inc(dots_copied[g % 2], 1)

        def copy_pair(eng, copy, u, j):
            eng.wait_ge(pair_transposed[j % 2], u * PP + j // 2 + 1)
            eng.wait_ge(pair_multiplied[j % 2], FREE + u * PP + j // 2)
            copy(eT[:, j % 2].rearrange("p a b c -> p (a b c)"), T_ps[j % 2][:]).then_inc(pair_copied[j % 2], 1)

        def copy_features(eng, copy, u, a):
            eng.wait_ge(features_transposed, FREE + FT * u + a + 1)
            for mp in range(2):
                src = M_ps[a][:, 0:P].rearrange("k (q mp t) -> k q mp t", q=QUADS, mp=2)[:, :, mp, :]
                last = copy(hT[:, a, mp, :].rearrange("k (q t) -> k q t", q=QUADS), src)
            last.then_inc(features_copied, 1)

        @block.scalar
        def _(act):
            act.dma_start(base_sb[:], first_row).then_inc(base_in, 16)
            act.dma_start(w1_sb[:, 0:KC // 2], w1[0:KC // 2 * P].rearrange("(c p) j -> p c j", p=P)).then_inc(w1_in, 16)
            act.dma_start(w1_sb[:, KC // 2:KC], w1[KC // 2 * P:].rearrange("(c p) j -> p c j", p=P)).then_inc(w1_in, 16)
            act.dma_start(w2_sb[:], w2.rearrange("(c p) j -> p c j", p=P)).then_inc(w23_in, 16)
            act.dma_start(w3_sb[:], w3).then_inc(w23_in, 16)
            act.dma_start(b1_sb[:], b1).then_inc(w23_in, 16)
            act.dma_start(b2_sb[:], b2).then_inc(w23_in, 16)
            for done in (pair_copied[1], *dots_copied):
                act.sem_inc(done, FREE)

            def relu(out, bank_, bias):
                return nc.scalar.activation(out, bank_[:, 0:UNIT], ACT.Relu, bias=bias)

            def mlp_step(u, step):
                if step == FEATURES:
                    copy_features(act, nc.scalar.copy, u, 1)
                if step in (LAYER1_LOW, LAYER1_HIGH):
                    jc = 2 * (step - LAYER1_LOW)
                    act.wait_ge(w23_in, 64)
                    act.wait_ge(layer1_summed, J1 * u + jc + 1)
                    relu(h1T[:, jc, :], l1_bank(jc), b1_sb[:, jc:jc + 1]).then_inc(h1_by_act, 1)
                if step == LAYER2:
                    act.wait_ge(layer2_summed, J2 * u + 1)
                    relu(h2T[:, 0, :], l2_bank(0), b2_sb[:, 0:1]).then_inc(h2_by_act, 1)

            def unit(u, one_before=True, two_before=True):
                for j in range(PAIRS):
                    if j % 2 == 1:
                        copy_pair(act, nc.scalar.copy, u, j)
                    elif j >= 2:
                        copy_dots(act, nc.scalar.copy, u, j // 2 - 1, (2, 3))
                    elif one_before:
                        copy_dots(act, nc.scalar.copy, u - 1, GROUPS - 1, (2, 3))
                    if j in (LAYER2, LAYER3):
                        if two_before:
                            mlp_step(u - 2, j)
                    elif one_before:
                        mlp_step(u - 1, j)

            unit(0, one_before=False, two_before=False)
            unit(1, two_before=False)
            with act.Fori(2, UNITS) as u:
                unit(u)
            copy_dots(act, nc.scalar.copy, UNITS - 1, GROUPS - 1, (2, 3))
            mlp_step(UNITS - 2, LAYER2)
            mlp_step(UNITS - 1, FEATURES)
            mlp_step(UNITS - 2, LAYER3)
            for step in (LAYER1_LOW, LAYER1_HIGH, LAYER2, LAYER3):
                mlp_step(UNITS - 1, step)

        @block.vector
        def _(dve):
            for done in (pair_copied[0], *dots_copied, z_made, z_dense, y_copied):
                dve.sem_inc(done, FREE)
            dve.wait_ge(base_in, 16)
            dve.wait_ge(ids_first_in, 16)
            nc.vector.tensor_scalar(stage[:], ids_sb[:, 0:TILES_U], base_sb[:, 0:1], None,
                                    ALU.add).then_inc(rows_made, 1)
            dve.wait_ge(ids_in, 16)
            nc.vector.tensor_scalar(rows_sb[:, TILES_U:], ids_sb[:, TILES_U:], base_sb[:, 0:1], None,
                                    ALU.add).then_inc(rows_made, 1)

            def relu(out, bank_, bias):
                return nc.vector.tensor_scalar(out, bank_[:, 0:UNIT], bias, 0.0, ALU.add, ALU.max)

            def make_z(u):
                dve.wait_ge(z_dense, FREE + u)
                nc.vector.tensor_copy(dense_now[:], dense_sb[:, bass.ds(u, 1), :]).then_inc(dense_copied, 1)
                for b in range(2):
                    dve.wait_ge(dots_copied[b], 2 * (FREE + (u + 1) * GP))
                dve.wait_ge(features_transposed, FREE + FT * u)
                nc.vector.transpose(z[:].rearrange("p m (mp t) -> p m mp t", mp=2),
                                    dots[:].rearrange("p t (m mp) -> p m mp t", mp=2)).then_inc(z_made, 1)
                high = z[:, MH // 2:, HALF:]
                dve.wait_ge(dense_copied, u + 1)
                dve.wait_ge(z_made, FREE + u + 1)
                dve.sem_inc(fold_steps, 1)
                nc.vector.copy_predicated(high, masks_sb[:, 1],
                                          dense_now[:].broadcast_to((P, HALF // 2, HALF))).then_inc(z_dense, 1)
                dve.wait_ge(z_dense, FREE + u + 1)
                dve.sem_inc(fold_steps, 1)
                nc.vector.copy_predicated(high, masks_sb[:, 0], z[:, 0:MH // 2, 0:HALF]).then_inc(z_folded, 1)

            def mlp_step(u, step):
                if step == FEATURES:
                    copy_features(dve, nc.vector.tensor_copy, u, 0)
                if step in (LAYER1_LOW, LAYER1_HIGH):
                    jc = 2 * (step - LAYER1_LOW) + 1
                    dve.wait_ge(w23_in, 64)
                    dve.wait_ge(layer1_summed, J1 * u + jc + 1)
                    relu(h1T[:, jc, :], l1_bank(jc), b1_sb[:, jc:jc + 1]).then_inc(h1_by_dve, 1)
                if step == LAYER2:
                    dve.wait_ge(layer2_summed, J2 * u + 2)
                    relu(h2T[:, 1, :], l2_bank(1), b2_sb[:, 1:2]).then_inc(h2_by_dve, 1)
                if step == LAYER3:
                    dve.wait_ge(layer3_summed, u + 1)
                    nc.vector.tensor_copy(y_sb[:, bass.ts(u, UNIT)], out_bank[0:1, 0:UNIT]).then_inc(y_copied, 1)

            dve.wait_ge(dense_in, 16)
            dve.wait_ge(masks_in, 16)

            def unit(u, one_before=True, two_before=True):
                for j in range(PAIRS):
                    if j % 2 == 0:
                        copy_pair(dve, nc.vector.tensor_copy, u, j)
                        if j >= 2:
                            copy_dots(dve, nc.vector.tensor_copy, u, j // 2 - 1, (0, 1))
                        elif one_before:
                            copy_dots(dve, nc.vector.tensor_copy, u - 1, GROUPS - 1, (0, 1))
                            make_z(u - 1)
                    if j in (LAYER2, LAYER3):
                        if two_before:
                            mlp_step(u - 2, j)
                    elif one_before:
                        mlp_step(u - 1, j)

            unit(0, one_before=False, two_before=False)
            unit(1, two_before=False)
            with dve.Fori(2, UNITS) as u:
                unit(u)
            copy_dots(dve, nc.vector.tensor_copy, UNITS - 1, GROUPS - 1, (0, 1))
            make_z(UNITS - 1)
            mlp_step(UNITS - 2, LAYER2)
            mlp_step(UNITS - 1, FEATURES)
            mlp_step(UNITS - 2, LAYER3)
            for step in (LAYER1_LOW, LAYER1_HIGH, LAYER2, LAYER3):
                mlp_step(UNITS - 1, step)


def feature_rows():
    import numpy as np

    pair = np.zeros((FIELDS, FIELDS), np.int64)
    iu, ju = np.triu_indices(FIELDS, k=1)
    pair[iu, ju] = pair[ju, iu] = np.arange(len(iu))
    rows = pair[HALF:, :].copy()
    for m in range(HALF):
        rows[m, HALF + m] = len(iu) + m
        rows[m, HALF + m + 1:] = pair[m, m + 1:HALF]
    return rows.reshape(2, QUADS, 2, FIELDS).transpose(0, 2, 1, 3).reshape(-1)


def fold_masks():
    import numpy as np

    mp = np.arange(P).reshape(P, 1, 1) // TILES_U % 2
    m = 2 * np.arange(HALF // 2).reshape(1, -1, 1) + mp
    n = np.arange(HALF).reshape(1, 1, -1)
    return np.stack([n > m, n == m], axis=1).astype(np.int32).reshape(P, -1)


def kernel(**inputs):
    import numpy as _np
    import concourse.bacc as _bacc
    from concourse import mybir as _mybir
    from concourse.bass_utils import run_bass_kernel_spmd as _run

    tables = [_np.asarray(inputs[f"tbl_{f}"]) for f in range(FIELDS)]
    starts = _np.cumsum([0] + [t.shape[0] for t in tables[:-1]]).astype(_np.int32)
    ids = _np.asarray(inputs["ids"])
    dense = _np.asarray(inputs["dense_ctx"])
    units = ids.shape[0] // UNIT
    arrays = {
        "table": _np.concatenate(tables, axis=0),
        "ids": _np.ascontiguousarray(ids.reshape(units, QUADS, TILES_U, FIELDS).transpose(1, 3, 0, 2).reshape(P, -1)),
        "first_row": _np.tile(starts, QUADS).reshape(P, 1),
        "dense": _np.repeat(dense.reshape(units, QUADS, 1, TILES_U, -1), 2, axis=2).transpose(1, 2, 3, 0, 4).reshape(P, -1),
        "masks": fold_masks(),
        "w1": _np.asarray(inputs["W_top1"])[feature_rows()],
        "b1": _np.ascontiguousarray(_np.asarray(inputs["b_top1"]).reshape(-1, P).T),
        "w2": _np.asarray(inputs["W_top2"]),
        "b2": _np.ascontiguousarray(_np.asarray(inputs["b_top2"]).reshape(-1, P).T),
        "w3": _np.ascontiguousarray(_np.asarray(inputs["W_top3"]).reshape(-1, P).T),
    }
    nc = _bacc.Bacc("TRN2", target_bir_lowering=False, num_devices=1)
    args = [nc.dram_tensor(n, a.shape, _mybir.dt.from_np(a.dtype), kind="ExternalInput").ap() for n, a in arrays.items()]
    out = nc.dram_tensor("y", (1, ids.shape[0]), _mybir.dt.float32, kind="ExternalOutput").ap()
    dlrm_tower_kernel(nc, *args, out)
    r = _run(nc, [arrays], core_ids=[0])
    return _np.asarray(r.results[0]["y"]).reshape(-1, 1)
```
